# Optimizing a Trainium2 kernel written in Bass

```python
import numpy as np
import jax
import jax.numpy as jnp

def _softmax(x, axis=-1):
    return jax.nn.softmax(x, axis=axis)

def _gelu(x):
    return jax.nn.gelu(x, approximate=True)

def _silu(x):
    return jax.nn.silu(x)

def _sigmoid(x):
    return jax.nn.sigmoid(x)

def _layernorm(x, axis=-1, eps=1e-05):
    m = jnp.mean(x, axis=axis, keepdims=True)
    v = jnp.var(x, axis=axis, keepdims=True)
    return (x - m) / jnp.sqrt(v + eps)

def _scatter_add(tgt, idx, src, axis=0):
    return tgt.at[idx].add(src)

def _segment_sum(src, seg, n):
    return jax.ops.segment_sum(src, seg, n)
kernel_name = 'mk_seq_postln_d1_jaxref_r2_a32420'

def setup_inputs(seed: int=0):
    np.random.seed(seed)
    _w = jnp.asarray

    def _L0_attn_setup():
        import math
        import jax, jax.numpy as jnp
        import numpy as np
        B, L, D = (4, 2048, 512)
        HID, PE, SHORT = (64, 3, 3)
        WIDTH = 3 * D

        def _gen_filter(length, W1, b1, f1, W2, b2, f2, W3, b3):
            t = jnp.arange(length, dtype=jnp.float32) / (length - 1)
            ang = 2.0 * math.pi * jnp.arange(length, dtype=jnp.float32) / length
            phase = 0.0001 * ang
            pe = jnp.stack([t, jnp.cos(phase), -jnp.sin(phase)], axis=-1)
            h = jnp.sin((pe @ W1 + b1) * f1)
            h = jnp.sin((h @ W2 + b2) * f2)
            k = h @ W3 + b3
            dmax, dmin = (math.log(0.01) / 0.3, math.log(0.01) / 1.5)
            deltas = jnp.abs(jnp.linspace(dmax, dmin, D).astype(jnp.float32))
            return k * jnp.exp(-t[:, None] * deltas[None, :])

        def _causal_fft_conv(v, k, bias):
            length = v.shape[1]
            n = 2 * length
            vp = jnp.pad(v, ((0, 0), (length - 1, 0), (0, 0)))
            Vf = jnp.fft.rfft(vp, n=n, axis=1)
            Kf = jnp.fft.rfft(k, n=n, axis=0)
            out = jnp.fft.irfft(Vf * jnp.conj(Kf)[None], n=n, axis=1)[:, :length]
            return out + bias

        def _short_conv(u, w, b):
            length = u.shape[1]
            up = jnp.pad(u, ((0, 0), (2, 2), (0, 0)))
            out = up[:, 0:length] * w[:, 0] + up[:, 1:length + 1] * w[:, 1] + up[:, 2:length + 2] * w[:, 2]
            return out + b
        key = jax.random.key(seed)
        ks = jax.random.split(key, 12)

        def nrm(k, shape, s):
            return jax.random.normal(k, shape, jnp.float32) * s
        return {'x': jax.random.normal(ks[0], (B, L, D), jnp.float32), 'W_in': nrm(ks[1], (D, WIDTH), 0.02), 'b_in': jnp.zeros((WIDTH,), jnp.float32), 'short_w': nrm(ks[2], (WIDTH, SHORT), 0.3), 'short_b': jnp.zeros((WIDTH,), jnp.float32), 'W1': nrm(ks[3], (PE, HID), 0.5), 'b1': jnp.zeros((HID,), jnp.float32), 'f1': jax.random.uniform(ks[4], (HID,), jnp.float32, 0.001, 10.0), 'W2': nrm(ks[5], (HID, HID), 0.3), 'b2': jnp.zeros((HID,), jnp.float32), 'f2': jax.random.uniform(ks[6], (HID,), jnp.float32, 0.001, 10.0), 'W3': nrm(ks[7], (HID, D), 0.3), 'b3': jnp.zeros((D,), jnp.float32), 'filter_bias': jnp.zeros((D,), jnp.float32), 'W_out': nrm(ks[8], (D, D), 0.02), 'b_out': jnp.zeros((D,), jnp.float32)}
    _L0_attn_in = _L0_attn_setup()

    def _L0_ffn_setup():
        import jax, jax.numpy as jnp
        import numpy as np
        DM = 512
        NEXPERTS = 32
        EXPERTSETS = 4
        EXPERTSIZE = 32
        BATCH, SEQ = (4, 1024)
        key = jax.random.key(seed)
        k0, k1, k2, k3 = jax.random.split(key, 4)
        scale = 0.02
        x = jax.random.normal(k0, (BATCH, SEQ, DM), jnp.float32)
        controller = jax.random.normal(k1, (DM, NEXPERTS, EXPERTSETS), jnp.float32) * scale
        f1 = jax.random.normal(k2, (DM, NEXPERTS, EXPERTSETS, EXPERTSIZE), jnp.float32) * scale
        bias = jnp.zeros((NEXPERTS, EXPERTSETS, EXPERTSIZE), jnp.float32)
        f2 = jax.random.normal(k3, (NEXPERTS, EXPERTSETS, EXPERTSIZE, DM), jnp.float32) * scale
        return {'x': x, 'controller': controller, 'f1': f1, 'bias': bias, 'f2': f2}
    _L0_ffn_in = _L0_ffn_setup()
    _d = {'L0_attn_x': _L0_attn_in['x'], 'L0_attn_W_in': _L0_attn_in['W_in'], 'L0_attn_b_in': _L0_attn_in['b_in'], 'L0_attn_short_w': _L0_attn_in['short_w'], 'L0_attn_short_b': _L0_attn_in['short_b'], 'L0_attn_W1': _L0_attn_in['W1'], 'L0_attn_b1': _L0_attn_in['b1'], 'L0_attn_f1': _L0_attn_in['f1'], 'L0_attn_W2': _L0_attn_in['W2'], 'L0_attn_b2': _L0_attn_in['b2'], 'L0_attn_f2': _L0_attn_in['f2'], 'L0_attn_W3': _L0_attn_in['W3'], 'L0_attn_b3': _L0_attn_in['b3'], 'L0_attn_filter_bias': _L0_attn_in['filter_bias'], 'L0_attn_W_out': _L0_attn_in['W_out'], 'L0_attn_b_out': _L0_attn_in['b_out'], 'L0_ffn_controller': _L0_ffn_in['controller'], 'L0_ffn_f1': _L0_ffn_in['f1'], 'L0_ffn_bias': _L0_ffn_in['bias'], 'L0_ffn_f2': _L0_ffn_in['f2']}
    _x0 = _d['L0_attn_x']
    _d['L0_attn_x'] = jax.random.normal(jax.random.fold_in(jax.random.key(seed), 1), (1, 8192, 512), dtype=_x0.dtype)
    del _x0
    return _d

def reference(L0_attn_x, L0_attn_W_in, L0_attn_b_in, L0_attn_short_w, L0_attn_short_b, L0_attn_W1, L0_attn_b1, L0_attn_f1, L0_attn_W2, L0_attn_b2, L0_attn_f2, L0_attn_W3, L0_attn_b3, L0_attn_filter_bias, L0_attn_W_out, L0_attn_b_out, L0_ffn_controller, L0_ffn_f1, L0_ffn_bias, L0_ffn_f2):

    def _L0_attn_ref(x, W_in, b_in, short_w, short_b, W1, b1, f1, W2, b2, f2, W3, b3, filter_bias, W_out, b_out):
        import math
        import jax, jax.numpy as jnp
        import numpy as np
        B, L, D = (4, 2048, 512)
        HID, PE, SHORT = (64, 3, 3)
        WIDTH = 3 * D

        def _gen_filter(length, W1, b1, f1, W2, b2, f2, W3, b3):
            t = jnp.arange(length, dtype=jnp.float32) / (length - 1)
            ang = 2.0 * math.pi * jnp.arange(length, dtype=jnp.float32) / length
            phase = 0.0001 * ang
            pe = jnp.stack([t, jnp.cos(phase), -jnp.sin(phase)], axis=-1)
            h = jnp.sin((pe @ W1 + b1) * f1)
            h = jnp.sin((h @ W2 + b2) * f2)
            k = h @ W3 + b3
            dmax, dmin = (math.log(0.01) / 0.3, math.log(0.01) / 1.5)
            deltas = jnp.abs(jnp.linspace(dmax, dmin, D).astype(jnp.float32))
            return k * jnp.exp(-t[:, None] * deltas[None, :])

        def _causal_fft_conv(v, k, bias):
            length = v.shape[1]
            n = 2 * length
            vp = jnp.pad(v, ((0, 0), (length - 1, 0), (0, 0)))
            Vf = jnp.fft.rfft(vp, n=n, axis=1)
            Kf = jnp.fft.rfft(k, n=n, axis=0)
            out = jnp.fft.irfft(Vf * jnp.conj(Kf)[None], n=n, axis=1)[:, :length]
            return out + bias

        def _short_conv(u, w, b):
            length = u.shape[1]
            up = jnp.pad(u, ((0, 0), (2, 2), (0, 0)))
            out = up[:, 0:length] * w[:, 0] + up[:, 1:length + 1] * w[:, 1] + up[:, 2:length + 2] * w[:, 2]
            return out + b
        u = x @ W_in + b_in
        uc = _short_conv(u, short_w, short_b)
        x0, x1, v = jnp.split(uc, 3, axis=-1)
        v = v * x1
        k = _gen_filter(x.shape[1], W1, b1, f1, W2, b2, f2, W3, b3)
        v = _causal_fft_conv(v, k, filter_bias)
        y = v * x0
        return y @ W_out + b_out

    def _L0_ffn_ref(x, controller, f1, bias, f2):
        import jax, jax.numpy as jnp
        import numpy as np
        DM = 512
        NEXPERTS = 32
        EXPERTSETS = 4
        EXPERTSIZE = 32
        BATCH, SEQ = (4, 1024)
        B, L, d = x.shape
        t = controller.shape[1]
        g = L // t
        grouped = x.reshape(B, g, t, d)
        logits = jnp.einsum('bgtd,des->bgtes', grouped, controller)
        tie = jnp.linspace(0.0, 1e-06, t, dtype=logits.dtype).reshape(t, 1, 1)
        logits = logits + tie
        perm = (logits == jnp.max(logits, axis=-3, keepdims=True)).astype(x.dtype)
        perm = jax.lax.stop_gradient(perm)
        dispatched = jnp.einsum('bgtd,bgtes->bgesd', grouped, perm)
        inner = jax.nn.relu(jnp.einsum('bgesd,desf->bgesf', dispatched, f1) + bias)
        intermediate = jnp.einsum('bgesf,esfd->bgesd', inner, f2)
        out = jnp.einsum('bgesd,bgtes->bgtd', intermediate, perm)
        return out.reshape(B, L, d)
    x = L0_attn_x
    x = _layernorm(x + _L0_attn_ref(x, L0_attn_W_in, L0_attn_b_in, L0_attn_short_w, L0_attn_short_b, L0_attn_W1, L0_attn_b1, L0_attn_f1, L0_attn_W2, L0_attn_b2, L0_attn_f2, L0_attn_W3, L0_attn_b3, L0_attn_filter_bias, L0_attn_W_out, L0_attn_b_out), axis=-1)
    x = _layernorm(x + _L0_ffn_ref(x, L0_ffn_controller, L0_ffn_f1, L0_ffn_bias, L0_ffn_f2), axis=-1)
    return x

_drawn_inputs = setup_inputs


def setup_inputs(seed=0):
    import zlib

    import numpy as np

    out = dict(_drawn_inputs(seed))
    spreads = {'L0_attn_b_in': (0.0, 0.1),
     'L0_attn_short_b': (0.0, 0.1),
     'L0_attn_b1': (0.0, 0.1),
     'L0_attn_b2': (0.0, 0.1),
     'L0_attn_b3': (0.0, 0.1),
     'L0_attn_filter_bias': (0.0, 0.516),
     'L0_attn_b_out': (0.0, 0.1),
     'L0_ffn_bias': (0.0, 0.518)}
    factors = {}
    for name, (base, spread) in spreads.items():
        noise = np.random.default_rng([zlib.crc32(name.encode()), seed]).standard_normal(out[name].shape)
        drawn = base * np.exp(spread * noise) if base else spread * noise
        out[name] = jnp.asarray(drawn.astype(out[name].dtype))
    for name, factor in factors.items():
        out[name] = (out[name] * factor).astype(out[name].dtype)
    return out
```

```python
from contextlib import ExitStack

import concourse.bass as bass
import numpy as np
from concourse import mybir

ALU = mybir.AluOpType
ACT = mybir.ActivationFunctionType
AX = mybir.AxisListType
F32 = mybir.dt.float32
F32R = mybir.dt.float32r
ds = bass.ds

P = 128
L = 8192
D = 512
DT = D // P
HID = 64
HE = HID + 1
CH = 512
NCH = L // CH
NB = CH // P

N = 2 * L
N2 = 64
N1 = L // N2
SLOTS = 128
SPITCH = 2 * N2 + 2
ZPITCH = 2 * SLOTS + 2

ES = 128
EF = 32
GT = 32
G = L // GT
NT = L // P
GC = 32
Q = ES // 4
EPS = 1e-5

ONE = 1


class Semaphores:

    def __init__(self, ctx, nc):
        self.ctx, self.nc, self.new = ctx, nc, []

    def __call__(self, name):
        self.new.append(self.ctx.enter_context(self.nc.semaphore(name)))
        return self.new[-1]

    def start(self, nc):
        new, self.new = self.new, []
        with nc.Block() as block:
            def inc(part):
                def _(eng):
                    for made in new[part::5]:
                        eng.sem_clear(made)
                        eng.sem_inc(made, ONE)
                return _

            for part, on in enumerate((block.sync, block.scalar, block.vector, block.tensor, block.gpsimd)):
                on(inc(part))


class Steps:

    def __init__(self, eng, sem, base=0):
        self.eng, self.sem, self.base, self.n = eng, sem, base, 0

    def __call__(self, ins):
        ins.then_inc(self.sem, 1)
        self.n += 1
        self.eng.wait_ge(self.sem, ONE + self.base + self.n)


class Norm:

    def __init__(self, nc, sem, sb, name, eps):
        self.nc, self.eps, self.eps_ok = nc, eps, sem(f"{name}_eps_ok")
        self.res = [sb(f"res{s}", [P, D]) for s in range(2)]
        self.stats = [sb(f"stats{s}", [P, 6]) for s in range(2)]
        self.mv = [sb(f"mv{s}", [P, 4]) for s in range(2)]
        self.std = [sb(f"std{s}", [P, 1]) for s in range(2)]
        self.res_ok, self.var_ok, self.std_ok, self.norm_ok, self.out_ok, self.stored = (
            [sem(f"{name}_{n}{s}") for s in range(2)] for n in
            ("res_ok", "var_ok", "std_ok", "norm_ok", "out_ok", "stored"))
        self.steps, self.passed = sem(f"{name}_nsteps"), sem(f"{name}_passed")

    def vector(self, dve, s, i, a, b, base):
        res, mv = self.res[s], self.mv[s]
        dve.wait_ge(self.stored[s], ONE + i * 16)
        dve.tensor_tensor(res[:], a[:], b[:], ALU.add).then_inc(self.res_ok[s], 1)
        dve.wait_ge(self.res_ok[s], ONE + i + 1)
        step = Steps(dve, self.steps, base)
        step(dve.bn_stats(self.stats[s][:], res[:]))
        dve.sem_inc(self.passed, 1)
        dve.bn_aggr(mv[:, 0:2], self.stats[s][:]).then_inc(self.var_ok[s], 1)
        dve.wait_ge(self.std_ok[s], ONE + i + 1)
        step(dve.reciprocal(mv[:, 2:3], self.std[s][:]))
        dve.tensor_scalar(mv[:, 3:4], mv[:, 0:1], mv[:, 2:3], -1.0, ALU.mult, ALU.mult).then_inc(self.norm_ok[s], 1)

    def scalar(self, act, s, i, dst):
        res, mv, nc = self.res[s], self.mv[s], self.nc
        act.wait_ge(self.var_ok[s], ONE + i + 1)
        nc.scalar.activation(self.std[s][:], mv[:, 1:2], ACT.Sqrt, bias=self.eps[:]).then_inc(self.std_ok[s], 1)
        act.wait_ge(self.norm_ok[s], ONE + i + 1)
        nc.scalar.activation(res[:], res[:], ACT.Identity, bias=mv[:, 3:4], scale=mv[:, 2:3]
                             ).then_inc(self.out_ok[s], 1)
        act.wait_ge(self.out_ok[s], ONE + i + 1)
        act.dma_start(dst, res[:]).then_inc(self.stored[s], 16)


def split_high(copy, high, x):
    return copy(high, x)


def split_low(eng, low, x, high):
    return eng.tensor_tensor(low, x, high.bitcast(F32), ALU.subtract)


def product(pe, out, a, b, start, stop):
    pe.matmul(out, a[0], b[0], start=start, stop=False)
    pe.matmul(out, a[1], b[0], start=False, stop=False)
    return pe.matmul(out, a[0], b[1], start=False, stop=stop)


def pipelined(eng, count, body):
    def step(j, off):
        def at(lag):
            s, use = (off + lag) % 2, j + (off + lag) // 2
            return (s, use) if not isinstance(j, int) or 0 <= 2 * use + s < count else None
        body(at)

    for n in range(-4, 2):
        step(n // 2, n % 2)
    with eng.Fori(1, count // 2 - 2) as j:
        step(j, 0)
        step(j, 1)
    for n in range(count - 4, count + 1):
        step(n // 2, n % 2)


def filter_phase(nc, sem, A, S):
    HALF = L // 2
    IT = HALF // CH
    with ExitStack() as ctx:
        def sb(name, shape):
            return ctx.enter_context(nc.sbuf_tensor(name, shape, F32))

        pos = sb("pos", [6, HALF])
        w1 = sb("w1", [6, P])
        w2 = sb("w2", [P, P])
        par = sb("par", [P, 4])
        ident = sb("f_ident", [P, P])
        arg = sb("arg", [P, CH])
        turns = sb("turns", [P, CH])
        red = sb("red", [P, CH])
        h1 = sb("h1", [P, CH])
        h2 = sb("h2", [P, CH])
        hout = sb("hout", [P, NB, 2, HE])
        pa = ctx.enter_context(nc.psum_tensor("f_pa", [P, CH], F32))
        pb = ctx.enter_context(nc.psum_tensor("f_pb", [P, CH], F32))
        pt = ctx.enter_context(nc.psum_tensor("f_pt", [P, NB, P], F32))

        loaded, zeroed = sem("f_loaded"), sem("f_zeroed")
        arg_ps, red_ok, h1_ok, arg2_ps, red2_ok, h2_ok = (sem(f"f_{n}") for n in (
            "arg_ps", "red_ok", "h1_ok", "arg2_ps", "red2_ok", "h2_ok"))
        turned, hout_ok, stored, chain = sem("f_turned"), sem("f_hout_ok"), sem("f_stored"), sem("f_chain")

        sem.start(nc)
        block = ctx.enter_context(nc.Block())

        @block.sync
        def _(sp):
            sp.wait_ge(zeroed, ONE + 3)
            for h in range(2):
                sp.dma_start(pos[3 * h:3 * h + 3, :], A["pos"][:, h * HALF:(h + 1) * HALF]).then_inc(loaded, 16)
                sp.dma_start(w1[3 * h:3 * h + 3, h * HID:(h + 1) * HID], A["W1"]).then_inc(loaded, 16)
                sp.dma_start(w2[h * HID:(h + 1) * HID, h * HID:(h + 1) * HID], A["W2"]).then_inc(loaded, 16)
                for j, n in enumerate(("b1", "f1", "b2", "f2")):
                    sp.dma_start(par[h * HID:(h + 1) * HID, j:j + 1],
                                 A[n].rearrange("(p a) -> p a", a=1)).then_inc(loaded, 16)
            sp.dma_start(ident[:], A["ident"]).then_inc(loaded, 16)
            dst = S["H"].rearrange("(h i b p) j -> h i p b j", h=2, i=IT, p=P)
            with sp.Fori(0, IT) as i:
                sp.wait_ge(hout_ok, ONE + i + 1)
                for h in range(2):
                    sp.dma_start(dst[h, ds(i, 1)].rearrange("a p b j -> p (a b) j"),
                                 hout[:, :, h, :]).then_inc(stored, 16)
            sp.wait_ge(stored, ONE + 32 * IT)

        @block.tensor
        def _(pe):
            pe.wait_ge(loaded, ONE + 16 * 15)
            with pe.Fori(0, IT) as i:
                pe.wait_ge(red_ok, ONE + i)
                pe.matmul(pa[:], w1[:], pos[:, ds(i * CH, CH)], start=True, stop=True).then_inc(arg_ps, 1)
                pe.wait_ge(h1_ok, ONE + i + 1)
                pe.matmul(pb[:], w2[:], h1[:], start=True, stop=True).then_inc(arg2_ps, 1)
                pe.wait_ge(h2_ok, ONE + i + 1)
                pe.wait_ge(hout_ok, ONE + i)
                for b in range(NB):
                    m = pe.transpose(pt[:, b, :], h2[:, b * P:(b + 1) * P], ident[:])
                m.then_inc(turned, 1)

        @block.scalar
        def _(act):
            with act.Fori(0, IT) as i:
                act.wait_ge(red_ok, ONE + i + 1)
                nc.scalar.activation(h1[:], red[:], ACT.Sin).then_inc(h1_ok, 1)
                act.wait_ge(red2_ok, ONE + i + 1)
                nc.scalar.activation(h2[:], red[:], ACT.Sin).then_inc(h2_ok, 1)

        @block.vector
        def _(dve):
            dve.memset(w1[:], 0.0).then_inc(zeroed, 1)
            dve.memset(w2[:], 0.0).then_inc(zeroed, 1)
            dve.memset(hout[:], 1.0).then_inc(zeroed, 1)
            dve.wait_ge(zeroed, ONE + 3)
            dve.wait_ge(loaded, ONE + 16 * 15)
            magic = float(1.5 * 2 ** 23)
            c1 = 6.28125
            c2 = float(np.float32(np.round((2 * np.pi - c1) * 2 ** 20) / 2 ** 20))
            c3 = float(np.float32(2 * np.pi - c1 - c2))
            pi = float(np.nextafter(np.float32(np.pi), np.float32(0)))

            def angles(step, src, b, f, done):
                step(dve.tensor_scalar(arg[:], src[:], par[:, b:b + 1], par[:, f:f + 1], ALU.add, ALU.mult))
                step(dve.tensor_scalar(turns[:], arg[:], float(1 / (2 * np.pi)), magic, ALU.mult, ALU.add))
                step(dve.tensor_scalar(turns[:], turns[:], magic, None, ALU.subtract))
                for c in (c1, c2, c3):
                    step(dve.scalar_tensor_tensor(arg[:], turns[:], -c, arg[:], ALU.mult, ALU.add))
                dve.tensor_scalar(red[:], arg[:], pi, -pi, ALU.min, ALU.max).then_inc(done, 1)

            with dve.Fori(0, IT) as i:
                step = Steps(dve, chain, i * 12)
                dve.wait_ge(arg_ps, ONE + i + 1)
                dve.wait_ge(h2_ok, ONE + i)
                angles(step, pa, 0, 1, red_ok)
                dve.wait_ge(arg2_ps, ONE + i + 1)
                dve.wait_ge(h1_ok, ONE + i + 1)
                dve.wait_ge(red_ok, ONE + i + 1)
                angles(step, pb, 2, 3, red2_ok)
                dve.wait_ge(turned, ONE + i + 1)
                dve.wait_ge(stored, ONE + i * 32)
                dve.wait_ge(red2_ok, ONE + i + 1)
                dve.tensor_copy(hout[:, :, :, 0:HID],
                                pt[:].rearrange("p b (h j) -> p b h j", h=2)).then_inc(hout_ok, 1)
                assert step.n == 12


def project_phase(nc, sem, A, S):
    with ExitStack() as ctx:
        def sb(name, shape):
            return ctx.enter_context(nc.sbuf_tensor(name, shape, F32))

        def ps(name):
            return ctx.enter_context(nc.psum_tensor(name, [P, CH], F32))

        W = 3 * DT
        ident = sb("p_ident", [P, P])
        win = sb("win", [P, DT, 3 * D])
        win_s = [ctx.enter_context(nc.sbuf_tensor(f"win_{n}", [P, DT, 3 * D], F32R)) for n in ("high", "low")]
        taps = sb("taps", [P, W, 3])
        bin_ = sb("bin", [P, W])
        sbias = sb("sbias", [P, W])
        tbias = sb("tbias", [P, W])
        damp = sb("damp", [P, DT, CH])
        damp_c = sb("damp_c", [P, DT, NCH])
        xT = [sb(f"xT{s}", [P, DT, CH]) for s in range(2)]
        xT_s = [[ctx.enter_context(nc.sbuf_tensor(f"xT_{n}{s}", [P, DT, CH], F32R)) for n in ("high", "low")]
                for s in range(2)]
        u = [sb(f"u{r}", [P, CH + 2]) for r in range(3)]
        halo = [sb(f"halo{s}", [P, W, 2]) for s in range(2)]
        t = [[sb(f"t{r}_{s}", [P, CH]) for s in range(2)] for r in range(3)]
        vout = [sb(f"vout{s}", [P, NB, P]) for s in range(2)]
        pu = [ps(f"pu{r}") for r in range(3)]
        pv = [ps(f"pv{s}") for s in range(2)]

        loaded, ready = sem("p_loaded"), sem("p_ready")
        x_in = [sem(f"p_x_in{s}") for s in range(2)]
        u_ps, u_ok = [sem(f"p_u_ps{s}") for s in range(2)], sem("p_u_ok")
        w_high, w_low = sem("p_w_high"), sem("p_w_low")
        x_high = [sem(f"p_x_high{s}") for s in range(2)]
        x_low = [sem(f"p_x_low{s}") for s in range(2)]
        bias_step, chain, v_ok, v_turned = sem("p_bias_step"), sem("p_chain"), sem("p_v_ok"), sem("p_v_turned")
        vout_ok = sem("p_vout_ok")
        halo_ok = sem("p_halo_ok")
        x0_st = [sem(f"p_x0_st{s}") for s in range(2)]
        v_st = [sem(f"p_v_st{s}") for s in range(2)]

        PAIRS = NCH // 2
        PER = 7
        sem.start(nc)
        block = ctx.enter_context(nc.Block())

        @block.sync
        def _(sp):
            sp.dma_start(win[:], A["W_in"].rearrange("(k p) w -> p k w", p=P)).then_inc(loaded, 16)
            sp.dma_start(ident[:], A["ident"]).then_inc(loaded, 16)
            sp.dma_start(taps[:], A["short_w"].rearrange("(w p) k -> p w k", p=P)).then_inc(loaded, 16)
            sp.dma_start(bin_[:], A["b_in"]).then_inc(loaded, 16)
            sp.dma_start(sbias[:], A["short_b"]).then_inc(loaded, 16)
            sp.dma_start(damp[:], A["damp"]).then_inc(loaded, 16)
            sp.dma_start(damp_c[:], A["damp_c"]).then_inc(loaded, 16)
            src = A["xT"].rearrange("(k p) t -> p k t", p=P)
            x0d = S["X0"].rearrange("(k p) t -> k p t", p=P)
            vd = S["V"].rearrange("(c b p) (k d) -> c k p b d", b=NB, p=P, k=DT)

            def load(i, s):
                sp.dma_start(xT[s][:], src[:, :, ds((2 * i + s) * CH, CH)]).then_inc(x_in[s], 16)

            def pair(i, last):
                for s in range(2):
                    for k in range(DT):
                        m = s * DT + k
                        q = m % 2
                        sp.wait_ge(chain, ONE + (i * 2 * DT + m) * PER + 2)
                        sp.dma_start(x0d[k, :, ds((2 * i + s) * CH, CH)], t[0][q][:]).then_inc(x0_st[q], 16)
                        if k == DT - 1 and not last:
                            sp.wait_ge(x_low[s], ONE + i + 1)
                            load(i + 1, s)
                        sp.wait_ge(vout_ok, ONE + i * 2 * DT + m + 1)
                        sp.dma_start(vd[ds(2 * i + s, 1), k].rearrange("a p b d -> p (a b) d"),
                                     vout[q][:]).then_inc(v_st[q], 16)

            load(0, 0)
            load(0, 1)
            with sp.Fori(0, PAIRS - 1) as i:
                pair(i, False)
            pair(PAIRS - 1, True)
            for q in range(2):
                sp.wait_ge(x0_st[q], ONE + 16 * NCH * DT // 2)
                sp.wait_ge(v_st[q], ONE + 16 * NCH * DT // 2)

        @block.gpsimd
        def _(pool):
            with pool.Fori(0, PAIRS) as i:
                for s in range(2):
                    pool.wait_ge(x_high[s], ONE + i + 1)
                    pool.wait_ge(u_ps[s], ONE + i * 3 * DT)
                    split_low(pool, xT_s[s][1][:], xT[s][:], xT_s[s][0][:]).then_inc(x_low[s], 1)

        @block.tensor
        def _(pe):
            pe.wait_ge(loaded, ONE + 16 * 7)
            pe.wait_ge(w_low, ONE + DT)

            def turn_v(i, m):
                pe.wait_ge(v_ok, ONE + i * 2 * DT + m + 1)
                pe.wait_ge(vout_ok, ONE + i * 2 * DT + max(m - 1, 0))
                for b in range(NB):
                    o = pe.transpose(pv[m % 2][:, b * P:(b + 1) * P], t[2][m % 2][:, b * P:(b + 1) * P], ident[:])
                o.then_inc(v_turned, 1)

            with pe.Fori(0, PAIRS) as i:
                for s in range(2):
                    pe.wait_ge(x_low[s], ONE + i + 1)
                    for k in range(DT):
                        m = s * DT + k
                        for r in range(3):
                            w = r * DT + k
                            pe.wait_ge(u_ok, ONE + i * 6 * DT + max(m * 3 + r - 2, 0))
                            for c in range(DT):
                                o = product(pe, pu[r][:], [h[:, c, w * P:(w + 1) * P] for h in win_s],
                                            [h[:, c, :] for h in xT_s[s]], start=(c == 0), stop=(c == DT - 1))
                            o.then_inc(u_ps[s], 1)
                        if m:
                            turn_v(i, m - 1)
                turn_v(i, 2 * DT - 1)

        @block.scalar
        def _(act):
            act.wait_ge(loaded, ONE + 16 * 7)

            def high(i, s):
                act.wait_ge(x_in[s], ONE + i * 16 + 16)
                act.wait_ge(u_ps[s], ONE + i * 3 * DT)
                split_high(nc.scalar.copy, xT_s[s][0][:], xT[s][:]).then_inc(x_high[s], 1)

            def copy_v(i, m):
                act.wait_ge(v_turned, ONE + i * 2 * DT + m + 1)
                act.wait_ge(v_st[m % 2], ONE + (i * DT + m // 2) * 16)
                nc.scalar.copy(vout[m % 2][:], pv[m % 2][:].rearrange("p (b d) -> p b d", b=NB)
                               ).then_inc(vout_ok, 1)

            for c in range(DT):
                split_high(nc.scalar.copy, win_s[0][:, c, :], win[:, c, :]).then_inc(w_high, 1)
            high(0, 0)
            act.wait_ge(ready, ONE + 2)

            def pair(i, last):
                for s in range(2):
                    for k in range(DT):
                        m = s * DT + k
                        q = m % 2
                        if k == DT // 2:
                            if s == 0:
                                high(i, 1)
                            elif not last:
                                high(i + 1, 0)
                        for r in range(3):
                            n = m * 3 + r
                            w = r * DT + k
                            act.wait_ge(u_ps[s], ONE + i * 3 * DT + k * 3 + r + 1)
                            act.wait_ge(chain, ONE + (i * 2 * DT + m) * PER)
                            act.wait_ge(halo_ok, ONE + i * 6 * DT + s * 3 * DT)
                            nc.scalar.copy(u[r][:, 0:2], halo[s][:, w, :])
                            nc.scalar.activation(u[r][:, 2:], pu[r][:], ACT.Identity, bias=bin_[:, w:w + 1])
                            nc.scalar.activation(halo[1 - s][:, w, :], pu[r][:, CH - 2:], ACT.Identity,
                                                 bias=bin_[:, w:w + 1]).then_inc(halo_ok, 1)
                            if r == 0:
                                act.wait_ge(x0_st[q], ONE + (i * DT + m // 2) * 16)
                            if r == 2:
                                act.wait_ge(v_turned, ONE + i * 2 * DT + max(m - 1, 0))
                            nc.scalar.activation(t[r][q][:], pu[r][:], ACT.Identity, bias=tbias[:, w:w + 1],
                                                 scale=taps[:, w, 2:3]).then_inc(u_ok, 1)
                        if m:
                            copy_v(i, m - 1)
                copy_v(i, 2 * DT - 1)

            with act.Fori(0, PAIRS - 1) as i:
                pair(i, False)
            pair(PAIRS - 1, True)

        @block.vector
        def _(dve):
            dve.memset(halo[0][:], 0.0).then_inc(ready, 1)
            dve.wait_ge(loaded, ONE + 16 * 7)
            for c in range(DT):
                dve.wait_ge(w_high, ONE + c + 1)
                split_low(dve, win_s[1][:, c, :], win[:, c, :], win_s[0][:, c, :]).then_inc(w_low, 1)
            step = Steps(dve, bias_step)
            step(dve.tensor_tensor(tbias[:], bin_[:], taps[:, :, 2], ALU.mult))
            dve.tensor_tensor(tbias[:], tbias[:], sbias[:], ALU.add).then_inc(ready, 1)
            with dve.Fori(0, PAIRS) as i:
                for m in range(2 * DT):
                    k, q = m % DT, m % 2
                    step = Steps(dve, chain, (i * 2 * DT + m) * PER)
                    for r in range(3):
                        w = r * DT + k
                        dve.wait_ge(u_ok, ONE + i * 6 * DT + m * 3 + r + 1)
                        for tap in (1, 0):
                            step(dve.scalar_tensor_tensor(t[r][q][:], u[r][:, tap:tap + CH], taps[:, w, tap:tap + 1],
                                                          t[r][q][:], ALU.mult, ALU.add))
                    step(dve.scalar_tensor_tensor(t[2][q][:], t[2][q][:], damp_c[:, k, ds(2 * i + m // DT, 1)],
                                                  t[1][q][:], ALU.mult, ALU.mult))
                    dve.tensor_tensor(t[2][q][:], t[2][q][:], damp[:, k, :], ALU.mult).then_inc(v_ok, 1)
                    assert step.n == PER


def forward_outer_phase(nc, sem, A, S):
    J = 4
    NG = N2 // J
    with ExitStack() as ctx:
        def sb(name, shape):
            return ctx.enter_context(nc.sbuf_tensor("a_" + name, shape, F32))

        def ps(name, shape):
            return ctx.enter_context(nc.psum_tensor("a_" + name, shape, F32))

        vin = [sb(f"vin{s}", [P, J, D]) for s in range(2)]
        hin = [sb(f"hin{s}", [P, J, HE]) for s in range(2)]
        dft = [sb(f"dft{s}", [P, J, 2, P]) for s in range(2)]
        vout = [sb(f"vout{s}", [P, 2, J, D]) for s in range(2)]
        hout = [sb(f"hout{s}", [P, 2, J, HE]) for s in range(2)]
        p_re = [ps(f"p_re{b}", [P, D]) for b in range(2)]
        p_im = [ps(f"p_im{b}", [P, D]) for b in range(2)]
        p_h = [ps(f"p_h{b}", [P, 2, HE]) for b in range(2)]

        loaded = [sem(f"a_loaded{s}") for s in range(2)]
        stored = [sem(f"a_stored{s}") for s in range(2)]
        summed = [sem(f"a_summed{s}") for s in range(2)]
        re_out = [sem(f"a_re_out{b}") for b in range(2)]
        im_out = [sem(f"a_im_out{b}") for b in range(2)]
        sem.start(nc)
        block = ctx.enter_context(nc.Block())

        @block.sync
        def _(sp):
            v = S["V"].rearrange("(p g j) c -> g p j c", g=NG, j=J)
            h = S["H"].rearrange("(p g j) c -> g p j c", g=NG, j=J)
            f = A["dft1"].rearrange("p (g j) r k -> g p (j r k)", j=J)

            def load(i, s):
                g = 2 * i + s
                sp.dma_start(vin[s][:], v[ds(g, 1)].rearrange("a p j c -> p (a j) c")).then_inc(loaded[s], 16)
                sp.dma_start(hin[s][:], h[ds(g, 1)].rearrange("a p j c -> p (a j) c")).then_inc(loaded[s], 16)
                sp.dma_start(dft[s][:].rearrange("p j r k -> p (j r k)"),
                             f[ds(g, 1)].rearrange("a p m -> p (a m)")).then_inc(loaded[s], 16)

            def pair(i, last):
                for s in range(2):
                    if not last:
                        sp.wait_ge(summed[s], ONE + (i + 1) * J)
                        load(i + 1, s)
                    for b in range(2):
                        sp.wait_ge(re_out[b], ONE + i * J + (s + 1) * J // 2)
                        sp.wait_ge(im_out[b], ONE + i * J + (s + 1) * J // 2)
                    for r in range(2):
                        at = r * N2 + (2 * i + s) * J
                        sp.dma_start(S["SV"][:, ds(at, J), :], vout[s][:, r]).then_inc(stored[s], 16)
                        sp.dma_start(S["SH"][:, ds(at, J), :], hout[s][:, r]).then_inc(stored[s], 16)

            load(0, 0)
            load(0, 1)
            with sp.Fori(0, NG // 2 - 1) as i:
                pair(i, False)
            pair(NG // 2 - 1, True)
            for s in range(2):
                sp.wait_ge(stored[s], ONE + 64 * NG // 2)

        @block.tensor
        def _(pe):
            with pe.Fori(0, NG // 2) as i:
                for s in range(2):
                    pe.wait_ge(loaded[s], ONE + i * 48 + 48)
                    for j in range(J):
                        b, n = j % 2, i * J + (s * J + j) // 2
                        pe.wait_ge(re_out[b], ONE + n)
                        pe.wait_ge(im_out[b], ONE + n)
                        for r, bank in enumerate((p_re, p_im)):
                            pe.matmul(bank[b][:], dft[s][:, j, r, :], vin[s][:, j, :], start=True, stop=True)
                            m = pe.matmul(p_h[b][:, r, :], dft[s][:, j, r, :], hin[s][:, j, :],
                                          start=True, stop=True)
                        m.then_inc(summed[s], 1)

        @block.scalar
        def _(act):
            with act.Fori(0, NG // 2) as i:
                for s in range(2):
                    act.wait_ge(stored[s], ONE + i * 64)
                    for j in range(J):
                        b = j % 2
                        act.wait_ge(summed[s], ONE + i * J + j + 1)
                        nc.scalar.copy(vout[s][:, 0, j, :], p_re[b][:]).then_inc(re_out[b], 1)

        @block.vector
        def _(dve):
            with dve.Fori(0, NG // 2) as i:
                for s in range(2):
                    dve.wait_ge(stored[s], ONE + i * 64)
                    for j in range(J):
                        b = j % 2
                        dve.wait_ge(summed[s], ONE + i * J + j + 1)
                        dve.tensor_copy(hout[s][:, :, j, :], p_h[b][:])
                        dve.tensor_copy(vout[s][:, 1, j, :], p_im[b][:]).then_inc(im_out[b], 1)


def frequency_phase(nc, sem, A, S):
    with ExitStack() as ctx:
        def sb(name, shape, dt=F32):
            return ctx.enter_context(nc.sbuf_tensor("q_" + name, shape, dt))

        def halves(name, shape):
            return [sb(f"{name}_{n}", shape, F32R) for n in ("high", "low")]

        def ps(name, shape):
            return ctx.enter_context(nc.psum_tensor("q_" + name, shape, F32))

        fwd, fwd_h = sb("fwd", [P, 2, P]), sb("fwd_h", [P, 2, 2 * P])
        inv, w3 = sb("inv", [P, 4, P]), sb("w3", [HE, D])
        fwd_s, inv_s, w3_s = halves("fwd", [P, 2, P]), halves("inv", [P, 4, P]), halves("w3", [HE, D])
        av = [sb(f"av{s}", [P, D]) for s in range(2)]
        av_s = [halves(f"av{s}", [P, D]) for s in range(2)]
        ah = [sb(f"ah{s}", [P, HE]) for s in range(2)]
        v = [sb(f"v{s}", [P, D]) for s in range(2)]
        h_s = [halves(f"h{s}", [HE, 2 * P]) for s in range(2)]
        y = [sb(f"y{s}", [P, 2, D]) for s in range(2)]
        y_s = [halves(f"y{s}", [P, 2, D]) for s in range(2)]
        z = [sb(f"z{s}", [P, D]) for s in range(2)]
        pv = [ps(f"pv{s}", [P, D]) for s in range(2)]
        ph = ps("ph", [HE, 2 * P])
        pg = [ps(f"pg{r}", [P, D]) for r in range(2)]
        pz = [ps(f"pz{s}", [P, D]) for s in range(2)]

        consts, c_high, c_low = sem("q_consts"), sem("q_c_high"), sem("q_c_low")
        (loaded, a_high, a_low, v_ps, v_ok, h_ps, h_high, h_ok, g_ps, y_ok, y_high, y_low, y_low1, z_ps, z_ok,
         stored) = ([sem(f"q_{n}{s}") for s in range(2)] for n in
                    ("loaded", "a_high", "a_low", "v_ps", "v_ok", "h_ps", "h_high", "h_ok", "g_ps", "y_ok", "y_high",
                     "y_low", "y_low1", "z_ps", "z_ok", "stored"))
        USES = SLOTS // 2
        sem.start(nc)
        block = ctx.enter_context(nc.Block())

        @block.sync
        def _(sp):
            sp.dma_start(fwd[:], A["fwd"]).then_inc(consts, 16)
            sp.dma_start(fwd_h[:], A["fwd_h"]).then_inc(consts, 16)
            sp.dma_start(inv[:], A["inv"]).then_inc(consts, 16)
            sp.dma_start(w3[0:HID, :], A["W3"]).then_inc(consts, 16)
            sp.dma_start(w3[HID:HE, :], A["b3"].rearrange("(a c) -> a c", a=1)).then_inc(consts, 16)

            def body(at):
                if load := at(3):
                    s, i = load
                    sp.wait_ge(a_low[s], ONE + i)
                    sp.wait_ge(h_ps[s], ONE + i)
                    sp.dma_start(av[s][:], S["SV"][ds(2 * i + s, 1), 0:2 * N2, :].rearrange("a p c -> (a p) c")
                                 ).then_inc(loaded[s], 16)
                    sp.dma_start(ah[s][:], S["SH"][ds(2 * i + s, 1), :, :].rearrange("a p c -> (a p) c")
                                 ).then_inc(loaded[s], 16)
                if store := at(-1):
                    s, i = store
                    sp.wait_ge(z_ok[s], ONE + i + 1)
                    for r in range(2):
                        sp.dma_start(S["Z"][:, ds(r * SLOTS + 2 * i + s, 1), :].rearrange("n a c -> n (a c)"),
                                     z[s][r * N2:(r + 1) * N2, :]).then_inc(stored[s], 16)

            pipelined(sp, SLOTS, body)
            for s in range(2):
                sp.wait_ge(stored[s], ONE + 32 * USES)

        @block.tensor
        def _(pe):
            pe.wait_ge(c_low, ONE + 3)
            pe.wait_ge(consts, ONE + 16 * 5)

            def transform(s, i, kind):
                pe.wait_ge(a_low[s], ONE + i + 1)
                pe.wait_ge(loaded[s], ONE + i * 32 + 32)
                pe.wait_ge(v_ok[s], ONE + i)
                product(pe, pv[s][:], [f[:, kind, :] for f in fwd_s], [a[:] for a in av_s[s]], True, True
                        ).then_inc(v_ps[s], 1)
                pe.wait_ge(h_ok[1 - s], ONE + i + s)
                pe.matmul(ph[:], ah[s][:], fwd_h[:, kind, :], start=True, stop=True).then_inc(h_ps[s], 1)

            def filters(s, i):
                pe.wait_ge(h_ok[s], ONE + i + 1)
                pe.wait_ge(y_ok[1 - s], ONE + i + s)
                for r in range(2):
                    m = product(pe, pg[r][:], [h[:, r * P:(r + 1) * P] for h in h_s[s]], [w[:] for w in w3_s],
                                True, True)
                m.then_inc(g_ps[s], 1)

            def inverse(s, i, kind):
                pe.wait_ge(y_low[s], ONE + i + 1)
                pe.wait_ge(y_low1[s], ONE + i + 1)
                pe.wait_ge(z_ok[s], ONE + i)
                for r in range(2):
                    m = product(pe, pz[s][:], [f[:, 2 * kind + r, :] for f in inv_s], [h[:, r, :] for h in y_s[s]],
                                r == 0, r == 1)
                m.then_inc(z_ps[s], 1)

            def body(at):
                def kind(slot):
                    return 0 if isinstance(slot[1], int) and slot == (0, 0) else 1

                if slot := at(1):
                    transform(*slot, kind(slot))
                if slot := at(0):
                    filters(*slot)
                if slot := at(-1):
                    inverse(*slot, kind(slot))

            pipelined(pe, SLOTS, body)

        @block.scalar
        def _(act):
            act.wait_ge(consts, ONE + 16 * 5)
            for high, x in ((fwd_s, fwd), (inv_s, inv), (w3_s, w3)):
                split_high(nc.scalar.copy, high[0][:], x[:]).then_inc(c_high, 1)

            def body(at):
                if slot := at(2):
                    s, i = slot
                    act.wait_ge(loaded[s], ONE + i * 32 + 32)
                    act.wait_ge(v_ps[s], ONE + i)
                    split_high(nc.scalar.copy, av_s[s][0][:], av[s][:]).then_inc(a_high[s], 1)
                if slot := at(1):
                    s, i = slot
                    act.wait_ge(v_ps[s], ONE + i + 1)
                    act.wait_ge(y_ok[s], ONE + i)
                    nc.scalar.copy(v[s][:], pv[s][:]).then_inc(v_ok[s], 1)
                if slot := at(0):
                    s, i = slot
                    act.wait_ge(y_ok[s], ONE + i + 1)
                    act.wait_ge(z_ps[s], ONE + i)
                    split_high(nc.scalar.copy, y_s[s][0][:], y[s][:]).then_inc(y_high[s], 1)
                if slot := at(-1):
                    s, i = slot
                    act.wait_ge(z_ps[s], ONE + i + 1)
                    act.wait_ge(stored[s], ONE + i * 32)
                    nc.scalar.copy(z[s][:], pz[s][:]).then_inc(z_ok[s], 1)

            pipelined(act, SLOTS, body)

        @block.gpsimd
        def _(pool):
            def body(at):
                if slot := at(2):
                    s, i = slot
                    pool.wait_ge(a_high[s], ONE + i + 1)
                    split_low(pool, av_s[s][1][:], av[s][:], av_s[s][0][:]).then_inc(a_low[s], 1)
                if slot := at(0):
                    s, i = slot
                    pool.wait_ge(y_high[s], ONE + i + 1)
                    split_low(pool, y_s[s][1][:, 0, :], y[s][:, 0, :], y_s[s][0][:, 0, :]).then_inc(y_low[s], 1)

            pipelined(pool, SLOTS, body)

        @block.vector
        def _(dve):
            for n, (halves_, x) in enumerate(((fwd_s, fwd), (inv_s, inv), (w3_s, w3))):
                dve.wait_ge(c_high, ONE + n + 1)
                split_low(dve, halves_[1][:], x[:], halves_[0][:]).then_inc(c_low, 1)

            def body(at):
                if slot := at(1):
                    s, i = slot
                    dve.wait_ge(h_ps[s], ONE + i + 1)
                    dve.wait_ge(g_ps[s], ONE + i)
                    split_high(dve.tensor_copy, h_s[s][0][:], ph[:]).then_inc(h_high[s], 1)
                    dve.wait_ge(h_high[s], ONE + i + 1)
                    split_low(dve, h_s[s][1][:], ph[:], h_s[s][0][:]).then_inc(h_ok[s], 1)
                if slot := at(0):
                    s, i = slot
                    dve.wait_ge(g_ps[s], ONE + i + 1)
                    dve.wait_ge(v_ok[s], ONE + i + 1)
                    dve.wait_ge(y_low[s], ONE + i)
                    dve.wait_ge(y_low1[s], ONE + i)
                    dve.tensor_tensor(y[s][:, 0, :], pg[0][:], v[s][:], ALU.mult)
                    dve.tensor_tensor(y[s][:, 1, :], pg[1][:], v[s][:], ALU.mult).then_inc(y_ok[s], 1)
                    dve.wait_ge(y_high[s], ONE + i + 1)
                    split_low(dve, y_s[s][1][:, 1, :], y[s][:, 1, :], y_s[s][0][:, 1, :]).then_inc(y_low1[s], 1)

            pipelined(dve, SLOTS, body)


def output_phase(nc, sem, A, S):
    with ExitStack() as ctx:
        def sb(name, shape):
            return ctx.enter_context(nc.sbuf_tensor("o_" + name, shape, F32))

        def ps(name, shape):
            return ctx.enter_context(nc.psum_tensor("o_" + name, shape, F32))

        x0 = sb("x0", [P, DT, L])
        wout = sb("wout", [P, DT, D])
        grow, grow_c = sb("grow", [P, DT, P]), sb("grow_c", [P, DT, N2])
        fbias, bout, eps = sb("fbias", [P, DT]), sb("bout", [P, D]), sb("eps", [P, 1])
        zin = [sb(f"zin{s}", [P, 2, D]) for s in range(2)]
        idft = [sb(f"idft{s}", [P, 2, P]) for s in range(2)]
        xr = [sb(f"xr{s}", [P, D]) for s in range(2)]
        gate = [sb(f"gate{s}", [P, DT, P]) for s in range(2)]
        offs = [sb(f"offs{s}", [P, DT, P]) for s in range(2)]
        y = [sb(f"y{s}", [P, DT, P]) for s in range(2)]
        pc = [ps(f"pc{s}", [P, DT, P]) for s in range(2)]
        po = [ps(f"po{s}", [P, D]) for s in range(2)]

        norm = Norm(nc, sem, sb, "o", eps)
        consts = sem("o_consts")
        loaded, x_in, c_ps, gates, y_ok, o_ps, c_used, x_sum = (
            [sem(f"o_{n}{s}") for s in range(2)] for n in
            ("loaded", "x_in", "c_ps", "gates", "y_ok", "o_ps", "c_used", "x_sum"))
        ysteps = sem("o_ysteps")
        USES = N2 // 2
        NCONST = DT + 5
        sem.start(nc)
        block = ctx.enter_context(nc.Block())

        @block.sync
        def _(sp):
            x0d = S["X0"].rearrange("(k p) t -> k p t", p=P)
            sp.dma_start(wout[:], A["W_out"].rearrange("(k p) d -> p k d", p=P)).then_inc(consts, 16)
            sp.dma_start(grow[:], A["grow"]).then_inc(consts, 16)
            sp.dma_start(grow_c[:], A["grow_c"]).then_inc(consts, 16)
            sp.dma_start(fbias[:], A["filter_bias"]).then_inc(consts, 16)
            sp.dma_start(bout[:], A["b_out"].rearrange("(a d) -> a d", a=1).to_broadcast([P, D])).then_inc(consts, 16)
            for k in range(DT):
                sp.dma_start(x0[:, k, :], x0d[k]).then_inc(consts, 16)
            xd = A["x"].rearrange("a (p n) d -> (a n) p d", n=N2)
            with sp.Fori(0, USES) as i:
                for s in range(2):
                    n2 = 2 * i + s
                    sp.wait_ge(c_ps[s], ONE + i)
                    sp.dma_start(zin[s][:], S["Z"][ds(n2, 1), 0:2 * SLOTS, :].rearrange(
                        "a (r k) c -> (a k) r c", r=2)).then_inc(loaded[s], 16)
                    sp.dma_start(idft[s][:], A["idft2"][:, ds(n2, 1)].rearrange("k a r n -> k (a r) n")
                                 ).then_inc(loaded[s], 16)
                    sp.wait_ge(norm.res_ok[s], ONE + i)
                    sp.dma_start(xr[s][:], xd[ds(n2, 1)].rearrange("a p d -> (a p) d")).then_inc(x_in[s], 16)

        @block.gpsimd
        def _(pool):
            nc.gpsimd.memset(eps[:], EPS).then_inc(norm.eps_ok, 1)
            pool.wait_ge(consts, ONE + 16 * NCONST)
            with pool.Fori(0, USES) as i:
                for s in range(2):
                    n2 = 2 * i + s
                    pool.wait_ge(y_ok[s], ONE + i)
                    x0s = x0[:].rearrange("p k (n a) -> p k n a", a=N2)[:, :, :, ds(n2, 1)].rearrange(
                        "p k n a -> p k (n a)")
                    pool.tensor_tensor(gate[s][:], x0s, grow_c[:, :, ds(n2, 1)].to_broadcast([P, DT, P]), ALU.mult)
                    pool.tensor_tensor(offs[s][:], x0s, fbias[:].rearrange("p (k a) -> p k a", a=1).to_broadcast(
                        [P, DT, P]), ALU.mult).then_inc(gates[s], 1)
                    pool.wait_ge(x_in[s], ONE + i * 16 + 16)
                    pool.tensor_tensor(xr[s][:], xr[s][:], bout[:], ALU.add).then_inc(x_sum[s], 1)

        @block.tensor
        def _(pe):
            pe.wait_ge(consts, ONE + 16 * NCONST)

            def conv(s, i):
                pe.wait_ge(loaded[s], ONE + i * 32 + 32)
                pe.wait_ge(c_used[s], ONE + i)
                for k in range(DT):
                    for r in range(2):
                        m = pe.matmul(pc[s][:, k, :], zin[s][:, r, k * P:(k + 1) * P], idft[s][:, r, :],
                                      start=(r == 0), stop=(r == 1))
                m.then_inc(c_ps[s], 1)

            def out(s, i):
                pe.wait_ge(y_ok[s], ONE + i + 1)
                pe.wait_ge(norm.res_ok[s], ONE + i)
                for k in range(DT):
                    m = pe.matmul(po[s][:], y[s][:, k, :], wout[:, k, :], start=(k == 0), stop=(k == DT - 1))
                m.then_inc(o_ps[s], 1)

            conv(0, 0)
            with pe.Fori(0, USES - 1) as i:
                conv(1, i)
                out(0, i)
                conv(0, i + 1)
                out(1, i)
            conv(1, USES - 1)
            out(0, USES - 1)
            out(1, USES - 1)

        @block.vector
        def _(dve):
            def gated(s, i, base):
                dve.wait_ge(c_ps[s], ONE + i + 1)
                dve.wait_ge(gates[s], ONE + i + 1)
                dve.wait_ge(o_ps[s], ONE + i)
                step = Steps(dve, ysteps, base)
                ins = dve.tensor_tensor(y[s][:], pc[s][:], grow[:], ALU.mult)
                ins.then_inc(c_used[s], 1)
                dve.wait_ge(c_used[s], ONE + i + 1)
                step(dve.tensor_tensor(y[s][:], y[s][:], gate[s][:], ALU.mult))
                dve.tensor_tensor(y[s][:], y[s][:], offs[s][:], ALU.add).then_inc(y_ok[s], 1)

            def normed(s, i):
                dve.wait_ge(o_ps[s], ONE + i + 1)
                dve.wait_ge(x_sum[s], ONE + i + 1)
                norm.vector(dve, s, i, po[s], xr[s], 4 * i + 2 * s)

            dve.wait_ge(consts, ONE + 16 * NCONST)
            gated(0, 0, 0)
            with dve.Fori(0, USES - 1) as i:
                gated(1, i, 2 * i + 1)
                normed(0, i)
                gated(0, i + 1, 2 * i + 2)
                normed(1, i)
            gated(1, USES - 1, 2 * USES - 1)
            normed(0, USES - 1)
            normed(1, USES - 1)

        @block.scalar
        def _(act):
            dst = S["X1"].rearrange("(p n) d -> n p d", n=N2)
            act.wait_ge(norm.eps_ok, ONE + 1)
            with act.Fori(0, USES) as i:
                for s in range(2):
                    norm.scalar(act, s, i, dst[ds(2 * i + s, 1)].rearrange("a p d -> (a p) d"))
            for s in range(2):
                act.wait_ge(norm.stored[s], ONE + 16 * USES)


def router_phase(nc, sem, A, S):
    with ExitStack() as ctx:
        def sb(name, shape):
            return ctx.enter_context(nc.sbuf_tensor("r_" + name, shape, F32))

        def ps(name, shape):
            return ctx.enter_context(nc.psum_tensor("r_" + name, shape, F32))

        ident, ctrl, tie = sb("ident", [P, P]), sb("ctrl", [P, DT, ES]), sb("tie", [P, CH])
        xin = [sb(f"xin{s}", [P, NB, D]) for s in range(2)]
        xT = [sb(f"xT{s}", [P, DT, CH]) for s in range(2)]
        logit = [sb(f"logit{s}", [P, CH]) for s in range(2)]
        top = [sb(f"top{s}", [P, CH // GT]) for s in range(2)]
        take = [sb(f"take{s}", [P, CH]) for s in range(2)]
        took = [sb(f"took{s}", [P, NB, ES]) for s in range(2)]
        px = [ps(f"px{s}", [P, CH]) for s in range(2)]
        pl = [ps(f"pl{s}", [P, CH]) for s in range(2)]
        pt = [ps(f"pt{s}", [P, NB, ES]) for s in range(2)]

        consts, steps = sem("r_consts"), sem("r_steps")
        x_in, x_turned, xT_ok, l_ps, l_ok, take_ok, t_ps, took_ok, take_st, took_st = (
            [sem(f"r_{n}{s}") for s in range(2)] for n in
            ("x_in", "x_turned", "xT_ok", "l_ps", "l_ok", "take_ok", "t_ps", "took_ok", "take_st", "took_st"))
        USES = NCH // 2
        sem.start(nc)
        block = ctx.enter_context(nc.Block())

        @block.sync
        def _(sp):
            sp.dma_start(ident[:], A["ident"]).then_inc(consts, 16)
            sp.dma_start(ctrl[:], A["ffn_controller"].rearrange("(k p) e s -> p k (e s)", p=P)).then_inc(consts, 16)
            sp.dma_start(tie[:], A["tie"]).then_inc(consts, 16)
            src = S["X1"].rearrange("(c b p) d -> c p b d", b=NB, p=P)
            dst = S["TOOK"].rearrange("(c b p) e -> c p b e", b=NB, p=P)

            def load(i, s):
                sp.dma_start(xin[s][:], src[ds(2 * i + s, 1)].rearrange("a p b d -> p (a b) d")
                             ).then_inc(x_in[s], 16)

            def pair(i, last):
                for s in range(2):
                    c = 2 * i + s
                    if not last:
                        sp.wait_ge(x_turned[s], ONE + (i + 1) * DT)
                        load(i + 1, s)
                    sp.wait_ge(take_ok[s], ONE + i + 1)
                    sp.dma_start(S["TAKE"][:, ds(c * CH, CH)], take[s][:]).then_inc(take_st[s], 16)
                    sp.wait_ge(took_ok[s], ONE + i + 1)
                    sp.dma_start(dst[ds(c, 1)].rearrange("a p b e -> p (a b) e"), took[s][:]
                                 ).then_inc(took_st[s], 16)

            load(0, 0)
            load(0, 1)
            with sp.Fori(0, USES - 1) as i:
                pair(i, False)
            pair(USES - 1, True)
            for s in range(2):
                sp.wait_ge(take_st[s], ONE + 16 * USES)
                sp.wait_ge(took_st[s], ONE + 16 * USES)

        @block.tensor
        def _(pe):
            pe.wait_ge(consts, ONE + 48)

            def turn(s, i):
                pe.wait_ge(x_in[s], ONE + i * 16 + 16)
                for k in range(DT):
                    if k < 2:
                        pe.wait_ge(xT_ok[1 - s], ONE + (i + s) * DT)
                    else:
                        pe.wait_ge(xT_ok[s], ONE + i * DT + k - 1)
                    for b in range(NB):
                        m = pe.transpose(px[k % 2][:, b * P:(b + 1) * P], xin[s][:, b, k * P:(k + 1) * P], ident[:])
                    m.then_inc(x_turned[s], 1)

            def logits(s, i):
                pe.wait_ge(xT_ok[s], ONE + i * DT + DT)
                pe.wait_ge(l_ok[s], ONE + i)
                for k in range(DT):
                    m = pe.matmul(pl[s][:], ctrl[:, k, :], xT[s][:, k, :], start=(k == 0), stop=(k == DT - 1))
                m.then_inc(l_ps[s], 1)

            def turn_take(s, i):
                pe.wait_ge(take_ok[s], ONE + i + 1)
                pe.wait_ge(took_ok[s], ONE + i)
                for b in range(NB):
                    m = pe.transpose(pt[s][:, b, :], take[s][:, b * P:(b + 1) * P], ident[:])
                m.then_inc(t_ps[s], 1)

            turn(0, 0)
            logits(0, 0)
            with pe.Fori(0, USES - 1) as i:
                turn(1, i)
                logits(1, i)
                turn_take(0, i)
                turn(0, i + 1)
                logits(0, i + 1)
                turn_take(1, i)
            turn(1, USES - 1)
            logits(1, USES - 1)
            turn_take(0, USES - 1)
            turn_take(1, USES - 1)

        @block.scalar
        def _(act):
            def copy_x(s, i):
                act.wait_ge(l_ps[s], ONE + i)
                for k in range(DT):
                    act.wait_ge(x_turned[s], ONE + i * DT + k + 1)
                    nc.scalar.copy(xT[s][:, k, :], px[k % 2][:]).then_inc(xT_ok[s], 1)

            def copy_take(s, i):
                act.wait_ge(t_ps[s], ONE + i + 1)
                act.wait_ge(took_st[s], ONE + i * 16)
                nc.scalar.copy(took[s][:], pt[s][:]).then_inc(took_ok[s], 1)

            copy_x(0, 0)
            with act.Fori(0, USES - 1) as i:
                copy_x(1, i)
                copy_take(0, i)
                copy_x(0, i + 1)
                copy_take(1, i)
            copy_x(1, USES - 1)
            copy_take(0, USES - 1)
            copy_take(1, USES - 1)

        @block.vector
        def _(dve):
            dve.wait_ge(consts, ONE + 48)
            with dve.Fori(0, USES) as i:
                for s in range(2):
                    step = Steps(dve, steps, 2 * i + s)
                    dve.wait_ge(l_ps[s], ONE + i + 1)
                    dve.tensor_tensor(logit[s][:], pl[s][:], tie[:], ALU.add).then_inc(l_ok[s], 1)
                    dve.wait_ge(l_ok[s], ONE + i + 1)
                    by_group = logit[s][:].rearrange("p (g t) -> p g t", t=GT)
                    step(dve.tensor_reduce(top[s][:], by_group, AX.X, ALU.max))
                    dve.wait_ge(take_st[s], ONE + i * 16)
                    dve.wait_ge(t_ps[s], ONE + i)
                    dve.tensor_tensor(take[s][:].rearrange("p (g t) -> p g t", t=GT), by_group,
                                      top[s][:].rearrange("p (g a) -> p g a", a=1).to_broadcast([P, CH // GT, GT]),
                                      ALU.is_equal).then_inc(take_ok[s], 1)


def expert_phase(nc, sem, A, S):
    TC = GC * GT // P
    NC = G // GC
    U = 4
    NU = Q // U
    E = 4
    with ExitStack() as ctx:
        def sb(name, shape):
            return ctx.enter_context(nc.sbuf_tensor("e_" + name, shape, F32))

        def ps(name, shape):
            return ctx.enter_context(nc.psum_tensor("e_" + name, shape, F32))

        f1 = sb("f1", [P, DT, Q, P])
        bias = sb("bias", [P, Q])
        taken = sb("taken", [P, DT, E, Q, GC])
        xt = [sb(f"xt{s}", [P, D]) for s in range(2)]
        pick = [sb(f"pick{s}", [P, 4, ES]) for s in range(2)]
        f2 = [sb(f"f2{s}", [P, U, D]) for s in range(2)]
        raw = [sb(f"raw{s}", [P, U, P]) for s in range(2)]
        hid = [sb(f"hid{s}", [P, U, P]) for s in range(2)]
        out = [sb(f"out{s}", [P, U, D]) for s in range(2)]
        pd = [ps(f"pd{s}", [P, 4, ES]) for s in range(2)]
        ph = [ps(f"ph{s}", [P, U, P]) for s in range(2)]
        po = [ps(f"po{s}", [P, D]) for s in range(2)]

        consts, zeroed = sem("e_consts"), sem("e_zeroed")
        tile_in, tile_ps, taken_ok, f2_in, h_ps, raw_ok, hid_ok, o_ps, o_ok, stored = (
            [sem(f"e_{n}{s}") for s in range(2)] for n in
            ("tile_in", "tile_ps", "taken_ok", "f2_in", "h_ps", "raw_ok", "hid_ok", "o_ps", "o_ok", "stored"))
        sem.start(nc)
        block = ctx.enter_context(nc.Block())

        @block.sync
        def _(sp):
            sp.wait_ge(zeroed, ONE + 4)
            for k in range(DT):
                sp.dma_start(f1[:, k], A["ffn_f1"][k * P:(k + 1) * P]).then_inc(consts, 16)
            sp.dma_start(bias[:], A["ffn_bias"]).then_inc(consts, 16)
            xd = S["X1"].rearrange("(n p) d -> n p d", p=P)
            td = S["TOOK"].rearrange("(n p) e -> n p e", p=P)
            dst = S["I"].rearrange("(c g) (e q) d -> c e g q d", g=GC, e=E)

            def load_weights(c, b):
                s, use = b % 2, c * (NU // 2) + b // 2
                sp.wait_ge(o_ps[s], ONE + use * U)
                sp.dma_start(f2[s][:], A["ffn_f2"][:, b * U:(b + 1) * U, :]).then_inc(f2_in[s], 16)

            with sp.Fori(0, NC) as c:
                for t in range(TC):
                    s, use = t % 2, c * (TC // 2) + t // 2
                    n = c * TC + t
                    sp.wait_ge(tile_ps[s], ONE + use * DT)
                    sp.dma_start(xt[s][:], xd[ds(n, 1)].rearrange("a p d -> (a p) d")).then_inc(tile_in[s], 16)
                    for g in range(4):
                        r = slice(g * GT, (g + 1) * GT)
                        sp.dma_start(pick[s][r, g, :], td[ds(n, 1), r].rearrange("a p e -> (a p) e")
                                     ).then_inc(tile_in[s], 16)
                load_weights(c, 0)
                load_weights(c, 1)
                for b in range(NU):
                    if b + 2 < NU:
                        load_weights(c, b + 2)
                    for h in range(2):
                        sp.wait_ge(o_ok[h], ONE + c * Q // 2 + (b + 1) * U // 2)
                    for e in range(E):
                        sp.dma_start(dst[ds(c, 1), e, :, b * U:(b + 1) * U, :].rearrange("a g q d -> (a g) q d"),
                                     out[b % 2][e * GC:(e + 1) * GC]).then_inc(stored[b % 2], 16)
            for s in range(2):
                sp.wait_ge(stored[s], ONE + 16 * E * NC * NU // 2)

        @block.tensor
        def _(pe):
            pe.wait_ge(consts, ONE + 16 * (DT + 1))

            def dispatch(c, t):
                s, use = t % 2, c * (TC // 2) + t // 2
                pe.wait_ge(tile_in[s], ONE + use * 80 + 80)
                for k in range(DT):
                    pe.wait_ge(taken_ok[k % 2], ONE + c * TC * 2 + t * 2 + k // 2)
                    pe.matmul(pd[k % 2][:], xt[s][:, k * P:(k + 1) * P], pick[s][:], start=True, stop=True
                              ).then_inc(tile_ps[s], 1)

            def layer1(c, b):
                s, use = b % 2, c * (NU // 2) + b // 2
                pe.wait_ge(raw_ok[s], ONE + use * 4)
                for u in range(U):
                    q = b * U + u
                    for k in range(DT):
                        m = pe.matmul(ph[s][:, u, :], f1[:, k, q, :], taken[:, k, :, q, :],
                                      start=(k == 0), stop=(k == DT - 1))
                m.then_inc(h_ps[s], 1)

            def layer2(c, b):
                s, use = b % 2, c * (NU // 2) + b // 2
                pe.wait_ge(hid_ok[s], ONE + use + 1)
                pe.wait_ge(f2_in[s], ONE + use * 16 + 16)
                for u in range(U):
                    pe.wait_ge(o_ok[u % 2], ONE + c * Q // 2 + b * 2 + u // 2)
                    pe.matmul(po[u % 2][:], hid[s][:, u, :], f2[s][:, u, :], start=True, stop=True
                              ).then_inc(o_ps[s], 1)

            with pe.Fori(0, NC) as c:
                for t in range(TC):
                    dispatch(c, t)
                for k in range(2):
                    pe.wait_ge(taken_ok[k], ONE + (c + 1) * TC * 2)
                layer1(c, 0)
                for b in range(NU):
                    if b + 1 < NU:
                        layer1(c, b + 1)
                    layer2(c, b)

        def copy_tile(eng, copy, c, t, k):
            eng.wait_ge(tile_ps[t % 2], ONE + (c * (TC // 2) + t // 2) * DT + k + 1)
            copy(taken[:, k, :, :, t * 4:(t + 1) * 4].rearrange("p e q g -> p g (e q)"), pd[k % 2][:]
                 ).then_inc(taken_ok[k % 2], 1)

        def copy_out(eng, copy, c, b, u):
            s, use = b % 2, c * (NU // 2) + b // 2
            eng.wait_ge(o_ps[s], ONE + use * U + u + 1)
            eng.wait_ge(stored[s], ONE + use * 64)
            copy(out[s][:, u, :], po[u % 2][:]).then_inc(o_ok[u % 2], 1)

        @block.scalar
        def _(act):
            def hidden(c, b):
                s, use = b % 2, c * (NU // 2) + b // 2
                act.wait_ge(raw_ok[s], ONE + use * 4 + 4)
                act.wait_ge(o_ps[s], ONE + use * U)
                nc.scalar.activation(hid[s][:], raw[s][:], ACT.Relu).then_inc(hid_ok[s], 1)

            with act.Fori(0, NC) as c:
                for t in range(TC):
                    for k in range(0, DT, 2):
                        copy_tile(act, nc.scalar.copy, c, t, k)
                hidden(c, 0)
                for b in range(NU):
                    if b + 1 < NU:
                        hidden(c, b + 1)
                    for u in range(0, U, 2):
                        copy_out(act, nc.scalar.copy, c, b, u)

        @block.vector
        def _(dve):
            for s in range(2):
                dve.memset(pick[s][:], 0.0).then_inc(zeroed, 1)
                dve.memset(raw[s][:], 0.0).then_inc(zeroed, 1)
            dve.wait_ge(zeroed, ONE + 4)
            dve.wait_ge(consts, ONE + 16 * (DT + 1))

            def hidden(c, b):
                s, use = b % 2, c * (NU // 2) + b // 2
                dve.wait_ge(h_ps[s], ONE + use + 1)
                dve.wait_ge(hid_ok[s], ONE + use)
                for e in range(E):
                    r = slice(e * EF, (e + 1) * EF)
                    dve.tensor_tensor(raw[s][r, :, r], ph[s][r, :, r],
                                      bias[r, b * U:(b + 1) * U].rearrange("p (q a) -> p q a", a=1).to_broadcast(
                                          [EF, U, GC]), ALU.add).then_inc(raw_ok[s], 1)

            with dve.Fori(0, NC) as c:
                for t in range(TC):
                    for k in range(1, DT, 2):
                        copy_tile(dve, dve.tensor_copy, c, t, k)
                hidden(c, 0)
                for b in range(NU):
                    if b + 1 < NU:
                        hidden(c, b + 1)
                    for u in range(1, U, 2):
                        copy_out(dve, dve.tensor_copy, c, b, u)


def combine_phase(nc, sem, A, S):
    with ExitStack() as ctx:
        def sb(name, shape):
            return ctx.enter_context(nc.sbuf_tensor("c_" + name, shape, F32))

        inter = [sb(f"inter{s}", [P, 4, D]) for s in range(2)]
        take = [sb(f"take{s}", [P, P]) for s in range(2)]
        xr = [sb(f"xr{s}", [P, D]) for s in range(2)]
        eps = sb("eps", [P, 1])
        po = [ctx.enter_context(nc.psum_tensor(f"c_po{s}", [P, D], F32)) for s in range(2)]
        norm = Norm(nc, sem, sb, "c", eps)
        loaded = [sem(f"c_loaded{s}") for s in range(2)]
        o_ps = [sem(f"c_o_ps{s}") for s in range(2)]
        USES = NT // 2
        sem.start(nc)
        block = ctx.enter_context(nc.Block())

        @block.sync
        def _(sp):
            xd = S["X1"].rearrange("(n p) d -> n p d", p=P)
            with sp.Fori(0, USES) as i:
                for s in range(2):
                    n = 2 * i + s
                    sp.wait_ge(norm.res_ok[s], ONE + i)
                    sp.dma_start(inter[s][:], S["I"][ds(4 * n, 4)].rearrange("g e d -> e g d")
                                 ).then_inc(loaded[s], 16)
                    sp.dma_start(take[s][:], S["TAKE"][:, ds(n * P, P)]).then_inc(loaded[s], 16)
                    sp.dma_start(xr[s][:], xd[ds(n, 1)].rearrange("a p d -> (a p) d")).then_inc(loaded[s], 16)

        @block.gpsimd
        def _(pool):
            nc.gpsimd.memset(eps[:], EPS).then_inc(norm.eps_ok, 1)

        @block.tensor
        def _(pe):
            with pe.Fori(0, USES) as i:
                for s in range(2):
                    pe.wait_ge(loaded[s], ONE + i * 48 + 48)
                    pe.wait_ge(norm.res_ok[s], ONE + i)
                    for g in range(4):
                        r = slice(g * GT, (g + 1) * GT)
                        m = pe.matmul(po[s][r, :], take[s][:, r], inter[s][:, g, :], start=True, stop=True)
                    m.then_inc(o_ps[s], 1)

        @block.vector
        def _(dve):
            with dve.Fori(0, USES) as i:
                for s in range(2):
                    dve.wait_ge(o_ps[s], ONE + i + 1)
                    norm.vector(dve, s, i, po[s], xr[s], 4 * i + 2 * s)

        @block.scalar
        def _(act):
            dst = S["out"].rearrange("a (n p) d -> (a n) p d", p=P)
            act.wait_ge(norm.eps_ok, ONE + 1)
            with act.Fori(0, USES) as i:
                for s in range(2):
                    norm.scalar(act, s, i, dst[ds(2 * i + s, 1)].rearrange("a p d -> (a p) d"))
            for s in range(2):
                act.wait_ge(norm.stored[s], ONE + 16 * USES)


PHASES = [filter_phase, project_phase, forward_outer_phase, frequency_phase, output_phase,
          router_phase, expert_phase, combine_phase]


def program(nc, A, S, phases=None):
    for phase in phases or PHASES:
        with ExitStack() as ctx:
            phase(nc, Semaphores(ctx, nc), A, S)


def constants():
    f = np.float32
    c = {"ident": np.eye(P)}
    t = (np.arange(L, dtype=f) / f(L - 1)).astype(f)
    ang = (f(2.0 * np.pi) * np.arange(L, dtype=f) / f(L)).astype(f)
    phase = (f(0.0001) * ang).astype(f)
    c["pos"] = np.stack([t, np.cos(phase), -np.sin(phase)])[:, ::-1]
    delta = np.abs(np.linspace(np.log(0.01) / 0.3, np.log(0.01) / 1.5, D)).astype(f).astype(np.float64)
    dk = delta.reshape(DT, P).T[:, :, None]
    c["damp"] = np.exp(-dk * np.arange(CH) / (L - 1))
    c["damp_c"] = np.exp(-dk * np.arange(NCH) * CH / (L - 1))
    c["grow"] = np.exp(-dk * (1 - N2 * np.arange(N1) / (L - 1)))
    c["grow_c"] = np.exp(dk * np.arange(N2) / (L - 1))
    n1, n2, k1 = np.arange(N1)[:, None, None], np.arange(N2)[None, :, None], np.arange(SLOTS)[None, None, :]
    th = 2 * np.pi * ((N2 * n1 + n2) * k1 % N) / N
    alt = np.where(np.arange(N1) % 2, -1.0, 1.0)
    re, im = np.cos(th), -np.sin(th)
    im[:, :, 0] = alt[:, None]
    c["dft1"] = np.stack([re, im], axis=2)
    back = np.stack([2 * np.cos(th), -2 * np.sin(th)], axis=0) / 256
    back[0, :, :, 0] = 1 / 256
    back[1, :, :, 0] = alt[:, None] / 256
    c["idft2"] = back.transpose(3, 2, 0, 1)
    a = np.arange(N2)
    w = 2 * np.pi * (np.outer(a, a) % N2) / N2
    C, Sn = np.cos(w), np.sin(w)
    fwd = np.block([[C, -Sn], [Sn, C]])
    inv = np.block([[C, Sn], [-Sn, C]]) / N2
    fwd0 = np.zeros((P, P))
    inv0 = np.zeros((P, P))
    fwd0[:N2, 0] = 1
    fwd0[:N2, N2] = np.where(a % 2, -1.0, 1.0)
    inv0[0, :N2] = 1
    inv0[N2, :N2] = np.where(a % 2, -1.0, 1.0)
    for p in range(1, 32):
        v = 2 * np.pi * a * p / N2
        fwd0[:N2, p], fwd0[:N2, N2 + p] = np.cos(v), -np.sin(v)
        inv0[p, :N2], inv0[N2 + p, :N2] = 2 * np.cos(v), -2 * np.sin(v)
    for p in range(32, 64):
        v = 2 * np.pi * a * (128 + 256 * (p - 32)) / N
        fwd0[N2:, p], fwd0[N2:, N2 + p] = np.cos(v), -np.sin(v)
        inv0[p, N2:], inv0[N2 + p, N2:] = 2 * np.cos(v), -2 * np.sin(v)
    inv0 /= N2

    def doubled(f):
        return np.concatenate([f[:, :N2], f[:, :N2], f[:, N2:], f[:, N2:]], axis=1)

    def turned(b):
        return np.concatenate([b[N2:], -b[:N2]], axis=0)

    d0 = doubled(fwd0)
    d0[:, N2] = fwd0[:, N2]
    d0[:, 2 * N2] = d0[:, 3 * N2] = 0
    c["fwd"] = np.stack([fwd0, fwd], axis=1)
    c["fwd_h"] = np.stack([d0, doubled(fwd)], axis=1)
    c["inv"] = np.stack([inv0, turned(inv0), inv, turned(inv)], axis=1)
    c["tie"] = np.tile(np.linspace(0.0, 1e-06, GT, dtype=f), (P, CH // GT))
    return {k: np.ascontiguousarray(v.astype(f)) for k, v in c.items()}


SCRATCH = {"H": (L, HE), "V": (L, D), "X0": (D, L),
           "SV": (SLOTS, SPITCH, D), "SH": (SLOTS, 2 * N2, HE), "Z": (N2, ZPITCH, D), "X1": (L, D),
           "TAKE": (ES, L), "TOOK": (L, ES), "I": (G, ES, D)}

def laid_out(inputs):
    a = {name: np.asarray(v) for name, v in inputs.items()}

    def columns(v):
        return v.reshape(-1, P).T

    for name in ("b_in", "short_b", "filter_bias"):
        a["L0_attn_" + name] = columns(a["L0_attn_" + name])
    a["L0_attn_xT"] = a["L0_attn_x"][0].T
    a["L0_ffn_f1"] = a["L0_ffn_f1"].reshape(D, 4, Q, EF).transpose(0, 2, 1, 3).reshape(D, Q, P)
    a["L0_ffn_bias"] = a["L0_ffn_bias"].reshape(4, Q, EF).transpose(0, 2, 1).reshape(P, Q)
    a["L0_ffn_f2"] = a["L0_ffn_f2"].reshape(4, Q, EF, D).transpose(0, 2, 1, 3).reshape(P, Q, D)
    return {name: np.ascontiguousarray(v) for name, v in a.items()}


def build(nc, arrays, debug=(), phases=None):
    A, S = {}, {}
    for name, a in arrays.items():
        ap = nc.dram_tensor(f"in_{name}", a.shape, F32, kind="ExternalInput").ap()
        A[name.replace("L0_attn_", "").replace("L0_", "")] = ap
    for name, shape in SCRATCH.items():
        kind = "ExternalOutput" if name in debug else "Internal"
        S[name] = nc.dram_tensor("s_" + name, shape, F32, kind=kind).ap()
    S["out"] = nc.dram_tensor("out_0", (1, L, D), F32, kind="ExternalOutput").ap()
    program(nc, A, S, phases)


def kernel(**inputs):
    import concourse.bacc as bacc
    from concourse.bass_utils import run_bass_kernel_spmd

    nc = bacc.Bacc("TRN2", target_bir_lowering=False, num_devices=1)
    arrays = laid_out(inputs)
    arrays.update(constants())
    build(nc, arrays)
    r = run_bass_kernel_spmd(nc, [{f"in_{name}": a for name, a in arrays.items()}], core_ids=[0])
    return r.results[0]["out_0"]
```
